# Optimizing a Trainium2 kernel written in Bass

```python
import numpy as np
import jax
import jax.numpy as jnp

def _softmax(x, axis=-1):
    return jax.nn.softmax(x, axis=axis)

def _gelu(x):
    return jax.nn.gelu(x, approximate=True)

def _silu(x):
    return jax.nn.silu(x)

def _sigmoid(x):
    return jax.nn.sigmoid(x)

def _layernorm(x, axis=-1, eps=1e-05):
    m = jnp.mean(x, axis=axis, keepdims=True)
    v = jnp.var(x, axis=axis, keepdims=True)
    return (x - m) / jnp.sqrt(v + eps)

def _scatter_add(tgt, idx, src, axis=0):
    return tgt.at[idx].add(src)

def _segment_sum(src, seg, n):
    return jax.ops.segment_sum(src, seg, n)
kernel_name = 'mk_macaron_d1_jaxref_r8_a7ddfe'

def setup_inputs(seed: int=0):
    np.random.seed(seed)
    _w = jnp.asarray

    def _L0_attn_setup():
        import jax, jax.numpy as jnp
        import numpy as np
        H = 32
        DN = 128
        DR = 64
        DV = 128
        DQ = DN + DR
        HID = 512
        NEG_INF = -1e+30
        key = jax.random.key(seed)
        k0, k1, k2, k3 = jax.random.split(key, 4)
        B, S = (4, 128)
        hidden_states = jax.random.normal(k0, (B, S, HID), dtype=jnp.float32)
        wq = jax.random.normal(k1, (HID, H * DQ), dtype=jnp.float32) * 0.02
        wkv = jax.random.normal(k2, (HID, H * (DN + DV) + DR), dtype=jnp.float32) * 0.02
        wo = jax.random.normal(k3, (H * DV, HID), dtype=jnp.float32) * 0.02
        return {'hidden_states': hidden_states, 'wq': wq, 'wkv': wkv, 'wo': wo}
    _L0_attn_in = _L0_attn_setup()

    def _L0_ffn_setup():
        import jax, jax.numpy as jnp
        import numpy as np
        BATCH, SEQ, D = (2, 256, 512)
        K, TOPK, RANK = (64, 16, 16)
        ALPHA = 32.0
        SCALING = ALPHA / RANK
        key = jax.random.key(seed)
        k1, k2, k3, k4 = jax.random.split(key, 4)
        x = jax.random.normal(k1, (BATCH, SEQ, D), dtype=jnp.float32)
        A = jax.random.normal(k2, (K, RANK, D), dtype=jnp.float32) * 0.02
        B = jax.random.normal(k3, (K, D, RANK), dtype=jnp.float32) * 0.02
        Wr = jax.random.normal(k4, (K, D), dtype=jnp.float32) * 0.02
        return {'x': x, 'A': A, 'B': B, 'Wr': Wr}
    _L0_ffn_in = _L0_ffn_setup()
    _d = {'L0_attn_hidden_states': _L0_attn_in['hidden_states'], 'L0_attn_wq': _L0_attn_in['wq'], 'L0_attn_wkv': _L0_attn_in['wkv'], 'L0_attn_wo': _L0_attn_in['wo'], 'L0_ffn_A': _L0_ffn_in['A'], 'L0_ffn_B': _L0_ffn_in['B'], 'L0_ffn_Wr': _L0_ffn_in['Wr']}
    _x0 = _d['L0_attn_hidden_states']
    _d['L0_attn_hidden_states'] = jax.random.normal(jax.random.fold_in(jax.random.key(seed), 1), (4, 256, 512), dtype=_x0.dtype)
    del _x0
    return _d

def reference(L0_attn_hidden_states, L0_attn_wq, L0_attn_wkv, L0_attn_wo, L0_ffn_A, L0_ffn_B, L0_ffn_Wr):

    def _L0_attn_ref(hidden_states, wq, wkv, wo):
        import jax, jax.numpy as jnp
        import numpy as np
        H = 32
        DN = 128
        DR = 64
        DV = 128
        DQ = DN + DR
        HID = 512
        NEG_INF = -1e+30
        B, S, D = hidden_states.shape
        q = jnp.einsum('bsd,de->bse', hidden_states, wq).reshape(B, S, H, DQ)
        kv = jnp.einsum('bsd,de->bse', hidden_states, wkv)
        k = kv[..., :H * DN].reshape(B, S, H, DN)
        v = kv[..., H * DN:H * (DN + DV)].reshape(B, S, H, DV)
        scale = DQ ** (-0.5)
        scores = jnp.einsum('bqhd,bkhd->bhqk', q[..., :DN], k) * scale
        causal = jnp.tril(jnp.ones((S, S), dtype=bool))
        scores = jnp.where(causal[None, None], scores, NEG_INF)
        probs = jax.nn.softmax(scores, axis=-1)
        attn = jnp.einsum('bhqk,bkhd->bqhd', probs, v).reshape(B, S, H * DV)
        return jnp.einsum('bse,ed->bsd', attn, wo)

    def _L0_ffn_ref(x, A, B, Wr):
        import jax, jax.numpy as jnp
        import numpy as np
        BATCH, SEQ, D = (2, 256, 512)
        K, TOPK, RANK = (64, 16, 16)
        ALPHA = 32.0
        SCALING = ALPHA / RANK
        prefix = x.shape[:-1]
        xf = x.reshape(-1, x.shape[-1])
        N = xf.shape[0]
        scores = xf @ Wr.T
        top_vals, top_idx = jax.lax.top_k(scores, TOPK)
        gates = jax.nn.softmax(top_vals, axis=-1)
        G = jnp.zeros((N, K), xf.dtype).at[jnp.arange(N)[:, None], top_idx].set(gates)
        h = jnp.einsum('nd,krd->nkr', xf, A)
        out = jnp.einsum('nkr,kdr->nd', h * G[:, :, None], B)
        return (out * SCALING).reshape(*prefix, -1)
    x = L0_attn_hidden_states
    x = x + 0.5 * _L0_ffn_ref(_layernorm(x, axis=-1), L0_ffn_A, L0_ffn_B, L0_ffn_Wr)
    x = x + _L0_attn_ref(_layernorm(x, axis=-1), L0_attn_wq, L0_attn_wkv, L0_attn_wo)
    x = x + 0.5 * _L0_ffn_ref(_layernorm(x, axis=-1), L0_ffn_A, L0_ffn_B, L0_ffn_Wr)
    return x

_drawn_inputs = setup_inputs


def setup_inputs(seed=0):
    import zlib

    import numpy as np

    out = dict(_drawn_inputs(seed))
    spreads = {}
    factors = {'L0_attn_wq': 4.189, 'L0_ffn_A': 2.73, 'L0_ffn_Wr': 2.896}
    for name, (base, spread) in spreads.items():
        noise = np.random.default_rng([zlib.crc32(name.encode()), seed]).standard_normal(out[name].shape)
        drawn = base * np.exp(spread * noise) if base else spread * noise
        out[name] = jnp.asarray(drawn.astype(out[name].dtype))
    for name, factor in factors.items():
        out[name] = (out[name] * factor).astype(out[name].dtype)
    return out
```

```python
from contextlib import ExitStack

import concourse.bass as bass
from concourse import mybir

F32 = mybir.dt.float32
F32R = mybir.dt.float32r
ALU = mybir.AluOpType
ACT = mybir.ActivationFunctionType

P = 128
D = 512
KD = D // P
TOKENS = 1024
NT = TOKENS // P
SEQ = 256
HALF = TOKENS // 2
TH = NT // 2
HEADS = 32
DH = 128
PAIRS = HEADS // 2
EXPERTS = 64
RANK = 16
TOPK = 16
KR = EXPERTS * RANK
NR = KR // P
UPW = EXPERTS + KR
WARM = 10
DC = 4
CHUNKS = ((0, 384), (384, 768), (768, UPW))
EPS = 1e-5
SCALE = float(128 + 64) ** -0.5
MASKED = -1e30
TAKEN = -3.0e38
BIG = 3.0e38


def build_macaron(nc, x_in, up_w, down_w, wqk, wv, wo, out):
    ctx = ExitStack()
    with ctx:
        base = 2048
        where = {}

        def place(name, shape, dtype, at=None):
            nonlocal base
            size = 4
            for n in shape[1:]:
                size *= n
            off = base if at is None else at
            if at is None:
                base += -(-size // 32) * 32
            where[name] = off
            return nc.alloc_sbuf_tensor_at(name, shape, dtype, offset=off)

        x = place("x", [P, NT, D], F32)
        upT_hi = place("upT_hi", [P, KD, UPW], F32R)
        upT_lo = place("upT_lo", [P, KD, UPW], F32R)
        downT_hi = place("downT_hi", [P, NR, D], F32R)
        downT_lo = place("downT_lo", [P, NR, D], F32R)
        xnT_hi = place("xnT_hi", [P, KD, TOKENS], F32R)
        xnT_lo = place("xnT_lo", [P, KD, TOKENS], F32R)
        wqk_hi = place("wqk_hi", [P, 2, 2, KD, DH], F32R)
        wqk_lo = place("wqk_lo", [P, 2, 2, KD, DH], F32R)
        wv_hi = place("wv_hi", [P, KD, 2 * DH], F32R)
        wv_lo = place("wv_lo", [P, KD, 2 * DH], F32R)
        wo_hi = place("wo_hi", [P, 2, D], F32R)
        wo_lo = place("wo_lo", [P, 2, D], F32R)
        stage_vo = place("stage_vo", [P, 2 * D], F32)
        stage_qk = place("stage_qk", [P, 2 * D], F32)
        v_hi = place("v_hi", [P, TH, 2 * DH], F32R)
        v_lo = place("v_lo", [P, TH, 2 * DH], F32R)
        v_raw = place("v_raw", [P, TH, 2 * DH], F32)
        attT_hi = place("attT_hi", [P, 2, TOKENS], F32R)
        attT_lo = place("attT_lo", [P, 2, TOKENS], F32R)
        qT_raw = place("qT_raw", [P, 2, 2 * P], F32)
        qT_hi = place("qT_hi", [P, 2, 2 * P], F32R)
        qT_lo = place("qT_lo", [P, 2, 2 * P], F32R)
        kT_raw = place("kT_raw", [P, 2, 2 * P], F32)
        kT_hi = place("kT_hi", [P, 2, HALF], F32R)
        kT_lo = place("kT_lo", [P, 2, HALF], F32R)
        prob = place("prob", [P, 2, 3 * P], F32)
        pT_hi = place("pT_hi", [P, 2, 2 * P], F32R)
        pT_lo = place("pT_lo", [P, 2, 2 * P], F32R)
        pT_raw = place("pT_raw", [P, 2, P], F32)
        mask = place("mask", [P, 3 * P], F32)
        ident = place("ident", [P, P], F32)
        xn = place("xn", [P, D], F32)
        xa = place("xa", [P, D], F32)
        nmax = place("nmax", [P, 4], F32)
        rsum = place("rsum", [P, 4], F32)
        rinv = place("rinv", [P, 4], F32)
        scs = place("scs", [P, EXPERTS], F32)
        wk1 = place("wk1", [P, EXPERTS], F32)
        wk2 = place("wk2", [P, EXPERTS], F32)
        gexp = place("gexp", [P, EXPERTS], F32)
        gate = place("gate", [P, EXPERTS], F32)
        top_a = place("top_a", [P, 8], F32)
        top_b = place("top_b", [P, 8], F32)
        negm = place("negm", [P, 1], F32)
        gsum = place("gsum", [P, 1], F32)
        ginv = place("ginv", [P, 1], F32)
        half_neg = place("half_neg", [P, 1], F32)
        st = [place(f"st{i}", [P, 6], F32) for i in range(2)]
        mv = [place(f"mv{i}", [P, 2], F32) for i in range(2)]
        ve = [place(f"ve{i}", [P, 1], F32) for i in range(2)]
        rstd = [place(f"rstd{i}", [P, 1], F32) for i in range(2)]
        upT_raw = place("upT_raw", [P, KD, UPW], F32, at=where["wqk_hi"])
        downT_raw = place("downT_raw", [P, NR, D], F32, at=where["attT_hi"])
        hT_hi = place("hT_hi", [P, NR, P], F32R, at=where["v_hi"])
        hT_lo = place("hT_lo", [P, NR, P], F32R, at=where["v_lo"])
        hg = place("hg", [P, KR], F32, at=where["v_raw"])
        xT_hi = place("xT_hi", [P, KD, P], F32R, at=where["prob"])
        xT_lo = place("xT_lo", [P, KD, P], F32R, at=where["prob"] + 4 * KD * P)

        bank = [ctx.enter_context(nc.psum_tensor(f"bank{i}", [P, 512], F32)) for i in range(8)]
        sp, qp, kp, fp, pv = bank[0:2], bank[2], bank[3], bank[4:6], bank[6]
        eb, tb, fb, ub, lb = bank[0:2], bank[2], bank[3], bank[4:7], bank[7]

        names = """x0_loaded x1_loaded xr_loaded up0_loaded up1_loaded up2_loaded up3_loaded
            down0_loaded down1_loaded down2_loaded down3_loaded
            vo_loaded qk_loaded out_stored
            warm_zeroed consts_zeroed consts_ready half_ready
            up_hi up_split down_hi down_split
            stats_a stats_b var_a var_b vareps_a vareps_b rstd_a rstd_b xn_ready xa_ready
            xT_ready xT_hi_done xT_split xaT_ready xaT_hi_done xaT_split
            up_ready scs_ready route_step negm_ready gexp_ready ginv_ready hg_ready
            hT_ready hT_hi_done hT_split down_ready combined
            wv_hi_s wv_split wo_hi_s wo_split wqk_hi_s wqk0_split wqk1_split
            scores_ready smax_ready exp_done rinv_ready p_ready pT_ready pT_hi_done pT_split
            q_ready q_hi_done q_split k_ready k_hi_done k_split
            fill_ready v_hi_done fill_done av_ready av_hi_done av_split""".split()
        s = {n: ctx.enter_context(nc.semaphore(n)) for n in names}
        up_loaded = [s[f"up{k}_loaded"] for k in range(KD)]
        down_loaded = [s[f"down{c}_loaded"] for c in range(DC)]

        def down_chunk(tensor, c):
            return tensor[:, c * NR // DC:(c + 1) * NR // DC, :].rearrange("p k n -> p (k n)")

        def fill_before(p, j, first):
            if first and j <= 1:
                return 2 + 2 * j
            return 12 * p + (-2, 0, 4, 6)[j]

        def wait_alone(eng, sem, value):
            if not isinstance(value, int):
                value = eng.to_reg(value)
                eng.wait_ge(s["half_ready"], 1)
            eng.wait_ge(sem, value)

        def mm3(dst, a_hi, a_lo, b_hi, b_lo, first, last):
            nc.tensor.matmul(dst, a_hi, b_lo, start=first, stop=False)
            nc.tensor.matmul(dst, a_lo, b_hi, start=False, stop=False)
            return nc.tensor.matmul(dst, a_hi, b_hi, start=False, stop=last)

        def pe_ffn_transpose(pe, n):
            pe.wait_ge(s["xn_ready"], n + 1)
            for k in range(KD):
                last = nc.tensor.transpose(tb[:, k * P:(k + 1) * P], xn[:, k * P:(k + 1) * P], ident[:])
            last.then_inc(s["xT_ready"], 1)

        def pe_ffn_up_first(pe):
            pe.wait_ge(s["xT_split"], 1)
            for k in range(KD):
                pe.wait_ge(s["up_split"], k + 1)
                for c, (a, b) in enumerate(CHUNKS):
                    last = mm3(ub[c][:, 0:b - a], xT_hi[:, k, :], xT_lo[:, k, :],
                               upT_hi[:, k, a:b], upT_lo[:, k, a:b], k == 0, k == KD - 1)
                    if k == KD - 1:
                        last.then_inc(s["up_ready"], 1)

        def pe_ffn_up(pe, n, used=None):
            pe.wait_ge(s["xT_split"], n + 1)
            for c, (a, b) in enumerate(CHUNKS):
                if used is not None and c < 2:
                    pe.wait_ge(s["fill_done"], used - 1 + c)
                for k in range(KD):
                    last = mm3(ub[c][:, 0:b - a], xT_hi[:, k, :], xT_lo[:, k, :],
                               upT_hi[:, k, a:b], upT_lo[:, k, a:b], k == 0, k == KD - 1)
                last.then_inc(s["up_ready"], 1)

        def pe_ffn_gated_transpose(pe, n):
            for i in range(NR):
                c = next(c for c, (a, b) in enumerate(CHUNKS) if EXPERTS + (i + 1) * P <= b)
                if i == 0 or c != before:
                    pe.wait_ge(s["hg_ready"], 3 * n + c + 1)
                before = c
                last = nc.tensor.transpose(eb[i // 4][:, (i % 4) * P:(i % 4 + 1) * P],
                                           hg[:, i * P:(i + 1) * P], ident[:])
                if i % 4 == 3:
                    last.then_inc(s["hT_ready"], 1)

        def pe_ffn_down(pe, n, dst=fb, first=False, last_tile=False):
            if not first and not last_tile:
                pe.wait_ge(s["combined"], n)
            for i in range(NR):
                if first and i % 2 == 0:
                    pe.wait_ge(s["down_split"], i // 2 + 1)
                if i % 4 == 0:
                    pe.wait_ge(s["hT_split"], 2 * n + 1 + i // 4)
                last = mm3(dst[:, :], hT_hi[:, i, :], hT_lo[:, i, :],
                           downT_hi[:, i, :], downT_lo[:, i, :], i == 0, i == NR - 1)
            last.then_inc(s["down_ready"], 1)

        def pe_att_transpose(pe, t, first=False):
            pe.wait_ge(s["xa_ready"], t + 1)
            if not first:
                pe.wait_ge(s["xaT_split"], t)
            for k in range(KD):
                last = nc.tensor.transpose(lb[:, k * P:(k + 1) * P], xa[:, k * P:(k + 1) * P], ident[:])
            last.then_inc(s["xaT_ready"], 1)

        def pe_project(pe, j, qk, dst, done):
            head, half = j % 2, j // 2
            for k in range(KD):
                last = mm3(dst[:, :], wqk_hi[:, head, qk, k, :], wqk_lo[:, head, qk, k, :],
                           xnT_hi[:, k, half * HALF:(half + 1) * HALF],
                           xnT_lo[:, k, half * HALF:(half + 1) * HALF], k == 0, k == KD - 1)
            last.then_inc(done, 1)

        def pe_value(pe, half, ab, used, wait_bank=True):
            if wait_bank:
                pe.wait_ge(s["fill_done"], used - 1)
            for i in range(2):
                t = half * TH + 2 * ab + i
                for k in range(KD):
                    last = mm3(fp[ab][:, i * 256:(i + 1) * 256],
                               xnT_hi[:, k, t * P:(t + 1) * P], xnT_lo[:, k, t * P:(t + 1) * P],
                               wv_hi[:, k, :], wv_lo[:, k, :], k == 0, k == KD - 1)
            last.then_inc(s["fill_ready"], 1)

        def pe_output(pe, half, i, used):
            pe.wait_ge(s["fill_done"], used - 1)
            t = half * TH + i
            for h in range(2):
                last = mm3(fp[i % 2][:, :], attT_hi[:, h, t * P:(t + 1) * P],
                           attT_lo[:, h, t * P:(t + 1) * P], wo_hi[:, h, :], wo_lo[:, h, :],
                           h == 0, h == 1)
            last.then_inc(s["fill_ready"], 1)

        def pe_scores(pe, u, j):
            slot = j % 2
            pe.wait_ge(s["q_split"], u + 1)
            pe.wait_ge(s["k_split"], u + 1)
            for b in range(2):
                nc.tensor.matmul(sp[b][:, 0:P], qT_raw[:, slot, b * P:(b + 1) * P],
                                 kT_raw[:, slot, b * P:(b + 1) * P], start=True, stop=True)
                mm3(sp[b][:, P:3 * P], qT_hi[:, slot, b * P:(b + 1) * P],
                    qT_lo[:, slot, b * P:(b + 1) * P], kT_hi[:, slot, b * SEQ:(b + 1) * SEQ],
                    kT_lo[:, slot, b * SEQ:(b + 1) * SEQ], True, True).then_inc(s["scores_ready"], 1)

        def pe_prob_transpose(pe, u):
            for b in range(2):
                pe.wait_ge(s["p_ready"], 4 * u + 2 * b + 2)
                for i in range(3):
                    last = nc.tensor.transpose(sp[b][:, i * P:(i + 1) * P],
                                               prob[:, b, i * P:(i + 1) * P], ident[:])
                last.then_inc(s["pT_ready"], 1)

        def pe_attend(pe, u, j, first=False):
            head, half = j % 2, j // 2
            if not first:
                pe.wait_ge(s["av_split"], u)
            for b in range(2):
                pe.wait_ge(s["pT_split"], 2 * u + b + 1)
                tile = half * 2 + b
                cols = slice(head * DH, (head + 1) * DH)
                mm3(pv[:, b * SEQ:(b + 1) * SEQ], v_hi[:, tile, cols], v_lo[:, tile, cols],
                    pT_hi[:, b, :], pT_lo[:, b, :], True, False)
                last = nc.tensor.matmul(pv[:, b * SEQ + P:(b + 1) * SEQ], v_raw[:, tile, cols],
                                        pT_raw[:, b, :], start=False, stop=True)
            last.then_inc(s["av_ready"], 1)

        def pe_pair(pe, p, first=False, final=False):
            for j in range(4):
                u = 4 * p + j
                used = fill_before(p, j, first)
                pe_scores(pe, u, j)
                nj = (j + 1) % 4
                project = not (final and j == 3)
                if project:
                    if nj == 0:
                        pe.wait_ge(s["wqk0_split"], p + 2)
                    if nj == 1:
                        pe.wait_ge(s["wqk1_split"], p + 1)
                    if first and nj == 2:
                        pe.wait_ge(s["xaT_split"], NT)
                    pe_project(pe, nj, 0, qp, s["q_ready"])

                def fill(ab):
                    if j == 0:
                        if first and ab == 0:
                            pe.wait_ge(s["xaT_split"], NT)
                        pe_value(pe, 1, ab, used + ab)
                    elif j == 2 and not final:
                        if ab == 0:
                            pe.wait_ge(s["wv_split"], p + 2)
                        pe_value(pe, 0, ab, used + ab)
                    elif j == 1 and not first:
                        for i in (2 * ab, 2 * ab + 1):
                            pe_output(pe, 1, i, used + i)
                    elif j == 3:
                        if ab == 0:
                            pe.wait_ge(s["wo_split"], p + 1)
                        for i in (2 * ab, 2 * ab + 1):
                            pe_output(pe, 0, i, used + i - 2 * final)
                fill(0)
                pe_prob_transpose(pe, u)
                if project:
                    pe_project(pe, nj, 1, kp, s["k_ready"])
                fill(1)
                if j in (0, 2):
                    pe.wait_ge(s["fill_done"], used if j == 0 else fill_before(p, 1, first))
                pe_attend(pe, u, j, first and j == 0)

        def act_copy(dst, src):
            return nc.scalar.copy(dst, src)

        def act_down_hi(act, c):
            act.wait_ge(down_loaded[c], 16)
            act_copy(down_chunk(downT_hi, c), down_chunk(downT_raw, c)).then_inc(s["down_hi"], 1)

        def act_ffn_transposed(act, n):
            act.wait_ge(s["xT_ready"], n + 1)
            act_copy(xT_hi[:, :, :].rearrange("p k t -> p (k t)"), tb[:, :]).then_inc(s["xT_hi_done"], 1)

        def act_gated_transposed(act, n):
            for i in range(2):
                act.wait_ge(s["hT_ready"], 2 * n + i + 1)
                act_copy(hT_hi[:, 4 * i:4 * i + 4, :].rearrange("p k t -> p (k t)"),
                         eb[i][:, :]).then_inc(s["hT_hi_done"], 1)

        def act_gate_exp(act, n):
            act.wait_ge(s["negm_ready"], n + 1)
            nc.scalar.activation(gexp[:, :], scs[:, :], ACT.Exp, bias=negm[:, :],
                                 scale=1.0).then_inc(s["gexp_ready"], 1)

        def act_att_transposed(act, t):
            act.wait_ge(s["xaT_ready"], t + 1)
            act_copy(xnT_hi[:, :, bass.ds(t * P, P)],
                     lb[:, :].rearrange("p (k t) -> p k t", k=KD)).then_inc(s["xaT_hi_done"], 1)

        def act_exp(act, u):
            for b in range(2):
                for i, (a, e) in enumerate(((0, P), (P, 3 * P))):
                    c = 2 * b + i
                    act.wait_ge(s["smax_ready"], 4 * u + c + 1)
                    nc.scalar.activation(prob[:, b, a:e], prob[:, b, a:e], ACT.Exp,
                                         bias=nmax[:, c:c + 1], scale=-1.0,
                                         accum_out=rsum[:, c:c + 1]).then_inc(s["exp_done"], 1)

        def act_q(act, u, slot):
            act.wait_ge(s["q_ready"], u + 1)
            q = qp[:, :].rearrange("p (b i t) -> p b i t", b=2, i=2)
            act_copy(qT_raw[:, slot, :].rearrange("p (b t) -> p b t", b=2), q[:, :, 0, :])
            act_copy(qT_hi[:, slot, :].rearrange("p (b t) -> p b t", b=2),
                     q[:, :, 1, :]).then_inc(s["q_hi_done"], 1)

        def act_k(act, u, slot):
            act.wait_ge(s["k_ready"], u + 1)
            k = kp[:, :].rearrange("p (b i t) -> p b i t", b=2, i=2)
            act_copy(kT_raw[:, slot, :].rearrange("p (b t) -> p b t", b=2), k[:, :, 0, :])
            act_copy(kT_hi[:, slot, :], kp[:, :]).then_inc(s["k_hi_done"], 1)

        def act_value(act, half, ab, used):
            act.wait_ge(s["fill_ready"], used + 1)
            tile = half * 2 + ab
            act_copy(v_raw[:, tile, :], fp[ab][:, 256:512])
            act_copy(v_hi[:, tile, :], fp[ab][:, 0:256]).then_inc(s["v_hi_done"], 1)

        def act_prob_transposed(act, u):
            for b in range(2):
                act.wait_ge(s["pT_ready"], 2 * u + b + 1)
                act_copy(pT_raw[:, b, :], sp[b][:, 2 * P:3 * P])
                act_copy(pT_hi[:, b, :], sp[b][:, 0:2 * P]).then_inc(s["pT_hi_done"], 1)

        def act_attended(act, u, j):
            head, half = j % 2, j // 2
            act.wait_ge(s["av_ready"], u + 1)
            act_copy(attT_hi[:, head, half * HALF:(half + 1) * HALF], pv[:, :]).then_inc(s["av_hi_done"], 1)

        def act_pair(act, p, first=False, final=False):
            for j in range(4):
                u = 4 * p + j
                used = fill_before(p, j, first)
                nj = (j + 1) % 4
                act_exp(act, u)
                if not (final and j == 3):
                    act_q(act, u + 1, nj % 2)
                if j == 0 or (j == 2 and not final):
                    act_value(act, 1 if j == 0 else 0, 0, used)
                act_prob_transposed(act, u)
                if not (final and j == 3):
                    act_k(act, u + 1, nj % 2)
                if j == 0 or (j == 2 and not final):
                    act_value(act, 1 if j == 0 else 0, 1, used + 1)
                act_attended(act, u, j)

        def lo(dst, src, hi):
            return nc.vector.tensor_tensor(dst, src, hi.bitcast(F32), ALU.subtract)

        def dve_stats(dve, n, which, src):
            stats, var = (s["stats_a"], s["var_a"]) if which == 0 else (s["stats_b"], s["var_b"])
            nc.vector.bn_stats(st[which][:, :], src).then_inc(stats, 1)
            wait_alone(dve, stats, n + 1)
            nc.vector.bn_aggr(mv[which][:, :], st[which][:, :]).then_inc(var, 1)

        def dve_normalise(dve, n, which, src):
            dst, root, done = ((xn, s["rstd_a"], s["xn_ready"]) if which == 0
                               else (xa, s["rstd_b"], s["xa_ready"]))
            dve.wait_ge(root, n + 1)
            nc.vector.tensor_scalar(dst[:, :], src, mv[which][:, 0:1], rstd[which][:, :],
                                    ALU.subtract, ALU.mult).then_inc(done, 1)

        def dve_ffn_transposed(dve, n):
            dve.wait_ge(s["xT_hi_done"], n + 1)
            lo(xT_lo[:, :, :].rearrange("p k t -> p (k t)"), tb[:, :],
               xT_hi[:, :, :].rearrange("p k t -> p (k t)")).then_inc(s["xT_split"], 1)

        def dve_att_transposed(dve, t):
            dve.wait_ge(s["xaT_hi_done"], t + 1)
            lo(xnT_lo[:, :, bass.ds(t * P, P)], lb[:, :].rearrange("p (k t) -> p k t", k=KD),
               xnT_hi[:, :, bass.ds(t * P, P)]).then_inc(s["xaT_split"], 1)

        def dve_gated_transposed(dve, n):
            for i in range(2):
                dve.wait_ge(s["hT_hi_done"], 2 * n + i + 1)
                lo(hT_lo[:, 4 * i:4 * i + 4, :].rearrange("p k t -> p (k t)"), eb[i][:, :],
                   hT_hi[:, 4 * i:4 * i + 4, :].rearrange("p k t -> p (k t)")).then_inc(s["hT_split"], 1)

        def dve_route(dve, n):
            step = [5 * n]

            def chained(ins):
                ins.then_inc(s["route_step"], 1)
                step[0] = step[0] + 1
                wait_alone(dve, s["route_step"], step[0])
            dve.wait_ge(s["up_ready"], 3 * n + 1)
            chained(nc.vector.tensor_copy(scs[:, :], ub[0][:, 0:EXPERTS]))
            chained(nc.vector.max(top_a[:, :], scs[:, :]))
            nc.vector.tensor_scalar(negm[:, :], top_a[:, 0:1], -1.0, None, ALU.mult).then_inc(s["negm_ready"], 1)
            chained(nc.vector.match_replace(wk1[:, :], top_a[:, :], scs[:, :], TAKEN))
            chained(nc.vector.max(top_b[:, :], wk1[:, :]))
            chained(nc.vector.match_replace(wk2[:, :], top_b[:, :], wk1[:, :], TAKEN))
            dve.wait_ge(s["gexp_ready"], n + 1)
            nc.vector.scalar_tensor_tensor(gate[:, :], wk2[:, :], TAKEN, gexp[:, :], ALU.is_equal,
                                           ALU.mult, accum_out=gsum[:, :]).then_inc(s["scs_ready"], 1)
            dve.wait_ge(s["scs_ready"], n + 1)
            for c, (a, b) in enumerate(CHUNKS):
                a0 = max(a, EXPERTS)
                e0, ne = (a0 - EXPERTS) // RANK, (b - a0) // RANK
                dve.wait_ge(s["up_ready"], 3 * n + c + 1)
                nc.vector.tensor_tensor(
                    hg[:, e0 * RANK:(e0 + ne) * RANK].rearrange("p (e r) -> p e r", r=RANK),
                    ub[c][:, a0 - a:b - a].rearrange("p (e r) -> p e r", r=RANK),
                    gate[:, e0:e0 + ne].unsqueeze(2).to_broadcast([P, ne, RANK]), ALU.mult).then_inc(s["hg_ready"], 1)

        def dve_gate_inverse(dve, n):
            if not isinstance(n, int) or n > 0:
                dve.wait_ge(s["combined"], n)
            nc.vector.reciprocal(ginv[:, :], gsum[:, :]).then_inc(s["ginv_ready"], 1)

        def dve_combine(dve, n, t, src=fb):
            dve.wait_ge(s["down_ready"], n + 1)
            dve.wait_ge(s["ginv_ready"], n + 1)
            nc.vector.scalar_tensor_tensor(x[:, bass.ds(t, 1), :].rearrange("p o d -> p (o d)"), src[:, :], ginv[:, :],
                                           x[:, bass.ds(t, 1), :].rearrange("p o d -> p (o d)"),
                                           ALU.mult, ALU.add).then_inc(s["combined"], 1)

        def xt(t):
            return x[:, bass.ds(t, 1), :].rearrange("p o d -> p (o d)")

        def dve_softmax_max(dve, u):
            for b in range(2):
                wait_alone(dve, s["scores_ready"], 2 * u + b + 1)
                for i, (a, e) in enumerate(((0, P), (P, 3 * P))):
                    c = 2 * b + i
                    nc.vector.tensor_tensor_reduce(
                        out=prob[:, b, a:e], in0=sp[b][:, a:e], in1=mask[:, a:e], scale=-SCALE,
                        scalar=BIG, op0=ALU.add, op1=ALU.min,
                        accum_out=nmax[:, c:c + 1]).then_inc(s["smax_ready"], 1)

        def dve_normalise_probs(dve, u):
            for b in range(2):
                dve.wait_ge(s["exp_done"], 4 * u + 2 * b + 2)
                nc.vector.reciprocal(rinv[:, 2 * b:2 * b + 2], rsum[:, 2 * b:2 * b + 2]).then_inc(s["rinv_ready"], 1)
            for b in range(2):
                dve.wait_ge(s["rinv_ready"], 2 * u + b + 1)
                for i, (a, e) in enumerate(((0, P), (P, 3 * P))):
                    c = 2 * b + i
                    nc.vector.tensor_scalar(prob[:, b, a:e], prob[:, b, a:e], rinv[:, c:c + 1], None,
                                            ALU.mult).then_inc(s["p_ready"], 1)

        def dve_q(dve, u, slot):
            dve.wait_ge(s["q_hi_done"], u + 1)
            q = qp[:, :].rearrange("p (b i t) -> p b i t", b=2, i=2)
            lo(qT_lo[:, slot, :].rearrange("p (b t) -> p b t", b=2), q[:, :, 1, :],
               qT_hi[:, slot, :].rearrange("p (b t) -> p b t", b=2)).then_inc(s["q_split"], 1)

        def dve_k(dve, u, slot):
            dve.wait_ge(s["k_hi_done"], u + 1)
            lo(kT_lo[:, slot, :], kp[:, :], kT_hi[:, slot, :]).then_inc(s["k_split"], 1)

        def dve_value(dve, half, ab, v_used):
            dve.wait_ge(s["v_hi_done"], v_used + 1)
            tile = half * 2 + ab
            lo(v_lo[:, tile, :], fp[ab][:, 0:256], v_hi[:, tile, :]).then_inc(s["fill_done"], 1)

        def dve_output(dve, half, i, used):
            dve.wait_ge(s["fill_ready"], used + 1)
            t = half * TH + i
            nc.vector.tensor_tensor(x[:, t, :], fp[i % 2][:, :], x[:, t, :], ALU.add).then_inc(s["fill_done"], 1)

        def dve_prob_transposed(dve, u):
            for b in range(2):
                dve.wait_ge(s["pT_hi_done"], 2 * u + b + 1)
                lo(pT_lo[:, b, :], sp[b][:, 0:2 * P], pT_hi[:, b, :]).then_inc(s["pT_split"], 1)

        def dve_attended(dve, u, j):
            head, half = j % 2, j // 2
            cols = slice(half * HALF, (half + 1) * HALF)
            dve.wait_ge(s["av_hi_done"], u + 1)
            lo(attT_lo[:, head, cols], pv[:, :], attT_hi[:, head, cols]).then_inc(s["av_split"], 1)

        def dve_pair(dve, p, first=False, final=False):
            for j in range(4):
                u = 4 * p + j
                used = fill_before(p, j, first)
                v_used = 4 * p + 2 + (2 if j == 2 else 0)
                nj = (j + 1) % 4

                def fill(ab):
                    if j == 0:
                        dve_value(dve, 1, ab, v_used + ab)
                    elif j == 2 and not final:
                        dve_value(dve, 0, ab, v_used + ab)
                    elif j == 1 and not first:
                        for i in (2 * ab, 2 * ab + 1):
                            dve_output(dve, 1, i, used + i)
                    elif j == 3:
                        for i in (2 * ab, 2 * ab + 1):
                            dve_output(dve, 0, i, used + i - 2 * final)
                dve_softmax_max(dve, u)
                dve_normalise_probs(dve, u)
                if not (final and j == 3):
                    dve_q(dve, u + 1, nj % 2)
                fill(0)
                dve_prob_transposed(dve, u)
                if not (final and j == 3):
                    dve_k(dve, u + 1, nj % 2)
                else:
                    dve.wait_ge(s["fill_done"], used - 1)
                    dve_stats(dve, NT, 0, x[:, 0, :])
                fill(1)
                if final and j == 3:
                    dve_normalise(dve, NT, 0, x[:, 0, :])
                dve_attended(dve, u, j)

        def pool_rstd(pool, n, which):
            var, vareps, done = ((s["var_a"], s["vareps_a"], s["rstd_a"]) if which == 0
                                 else (s["var_b"], s["vareps_b"], s["rstd_b"]))
            wait_alone(pool, var, n + 1)
            nc.gpsimd.tensor_scalar(ve[which][:, :], mv[which][:, 1:2], EPS, 1.0, ALU.add,
                                    ALU.mult).then_inc(vareps, 1)
            pool.wait_ge(vareps, n + 1)
            nc.gpsimd.tensor_tensor(rstd[which][:, :], ve[which][:, :], half_neg[:, :],
                                    ALU.pow).then_inc(done, 1)

        def pool_split(pool, hi, lo_, raw, hi_done, hi_count, done):
            nc.gpsimd.tensor_copy(hi, raw).then_inc(hi_done, 1)
            pool.wait_ge(hi_done, hi_count)
            nc.gpsimd.tensor_tensor(lo_, raw, hi.bitcast(F32), ALU.subtract).then_inc(done, 1)

        def pool_wv(pool, p):
            pool_split(pool, wv_hi[:, :, :].rearrange("p k n -> p (k n)"),
                       wv_lo[:, :, :].rearrange("p k n -> p (k n)"), stage_vo[:, :],
                       s["wv_hi_s"], p + 1, s["wv_split"])

        def pool_wo(pool, p):
            pool_split(pool, wo_hi[:, :, :].rearrange("p k n -> p (k n)"),
                       wo_lo[:, :, :].rearrange("p k n -> p (k n)"), stage_vo[:, :],
                       s["wo_hi_s"], p + 1, s["wo_split"])

        def pool_wqk(pool, p, head):
            pool_split(pool, wqk_hi[:, head, :, :, :].rearrange("p q k n -> p (q k n)"),
                       wqk_lo[:, head, :, :, :].rearrange("p q k n -> p (q k n)"), stage_qk[:, :],
                       s["wqk_hi_s"], 2 * p + head + 1, s["wqk0_split"] if head == 0 else s["wqk1_split"])

        def pool_pair(pool, p, first=False, final=False):
            if not final:
                wait_alone(pool, s["fill_ready"], fill_before(p, 1, first))
                wait_alone(pool, s["vo_loaded"], 16 * (2 if first else 2 * p + 2))
                pool_wv(pool, p + 1)
            wait_alone(pool, s["fill_ready"], fill_before(p, 2, first))
            wait_alone(pool, s["vo_loaded"], 16 * (32 if final else (3 if first else 2 * p + 3)))
            pool_wo(pool, p)
            if not final:
                for head in range(2):
                    wait_alone(pool, s["k_ready"], 4 * p + 3 + head)
                    wait_alone(pool, s["qk_loaded"], 16 * (2 * p + 3 + head))
                    pool_wqk(pool, p + 1, head)

        def load_vo(sp_, src, p):
            sp_.dma_start(stage_vo[:, :], src[bass.ds(p, 1), :, :].rearrange("o p n -> (o p) n")).then_inc(s["vo_loaded"], 16)

        def load_qk(sp_, head):
            sp_.dma_start(stage_qk[:, :], wqk[bass.ds(head, 1), :, :].rearrange("o p n -> (o p) n")).then_inc(s["qk_loaded"], 16)

        def load_pair(sp_, p, first=False, final=False):
            if not final:
                if first:
                    sp_.wait_ge(s["wv_split"], 1)
                else:
                    sp_.wait_ge(s["wo_split"], p)
                load_vo(sp_, wv, p + 1)
                sp_.wait_ge(s["wqk1_split"], p + 1)
                load_qk(sp_, 2 * p + 2)
                sp_.wait_ge(s["wv_split"], p + 2)
            else:
                sp_.wait_ge(s["wo_split"], p)
            load_vo(sp_, wo, p)
            if not final:
                sp_.wait_ge(s["wqk0_split"], p + 2)
                load_qk(sp_, 2 * p + 3)

        block = ctx.enter_context(nc.Block())

        @block.sync
        def _(sync):
            sync.dma_start(x[:, 0, :], x_in[0]).then_inc(s["x0_loaded"], 16)
            for k in range(KD):
                sync.dma_start(upT_raw[:, k, :], up_w[:, k, :]).then_inc(up_loaded[k], 16)
            sync.dma_start(x[:, 1, :], x_in[1]).then_inc(s["x1_loaded"], 16)
            for c in range(DC):
                sync.dma_start(down_chunk(downT_raw, c),
                               down_chunk(down_w, c)).then_inc(down_loaded[c], 16)
            sync.dma_start(x[:, 2:NT, :], x_in[2:NT].rearrange("t p d -> p t d")).then_inc(s["xr_loaded"], 16)
            load_vo(sync, wv, 0)
            load_qk(sync, 0)
            sync.wait_ge(s["wqk0_split"], 1)
            load_qk(sync, 1)
            load_pair(sync, 0, first=True)
            with sync.Fori(1, PAIRS - 1) as p:
                load_pair(sync, p)
            load_pair(sync, PAIRS - 1, final=True)
            with sync.Fori(0, NT) as t:
                sync.wait_ge(s["combined"], NT + 1 + t)
                sync.dma_start(out[bass.ds(t, 1), :, :].rearrange("o p d -> (o p) d"), xt(t)).then_inc(s["out_stored"], 16)
            sync.wait_ge(s["out_stored"], 16 * NT)

        @block.gpsimd
        def _(pool):
            nc.gpsimd.memset(xa[:, 0:P], 0.0).then_inc(s["warm_zeroed"], 1)
            nc.gpsimd.memset(half_neg[:, :], -0.5).then_inc(s["half_ready"], 1)
            nc.gpsimd.memset(ident[:, :], 0.0).then_inc(s["consts_zeroed"], 1)
            nc.gpsimd.memset(mask[:, :], 0.0).then_inc(s["consts_zeroed"], 1)
            pool.wait_ge(s["half_ready"], 1)
            pool_rstd(pool, 0, 0)
            pool.wait_ge(s["consts_zeroed"], 2)
            nc.gpsimd.affine_select(out=ident[:, :], in_=ident[:, :], compare_op=ALU.not_equal, fill=1.0,
                                    base=0, pattern=[[-1, P]], channel_multiplier=1).then_inc(s["consts_ready"], 1)
            for c in (0, 2 * P):
                nc.gpsimd.affine_select(out=mask[:, c:c + P], in_=mask[:, c:c + P], compare_op=ALU.is_ge,
                                        fill=MASKED, base=0, pattern=[[-1, P]],
                                        channel_multiplier=1).then_inc(s["consts_ready"], 1)
            pool_rstd(pool, 1, 0)
            for c in range(DC):
                pool.wait_ge(s["down_hi"], c + 1)
                nc.gpsimd.tensor_tensor(down_chunk(downT_lo, c), down_chunk(downT_raw, c),
                                        down_chunk(downT_hi, c).bitcast(F32),
                                        ALU.subtract).then_inc(s["down_split"], 1)
            pool.wait_ge(s["up_split"], KD)
            pool_rstd(pool, 2, 0)
            pool_rstd(pool, 0, 1)
            pool_rstd(pool, 3, 0)
            pool.wait_ge(s["vo_loaded"], 16)
            pool_wv(pool, 0)
            pool_rstd(pool, 1, 1)
            pool_rstd(pool, 4, 0)
            pool.wait_ge(s["qk_loaded"], 16)
            pool_wqk(pool, 0, 0)
            with pool.Fori(2, NT - 3) as t:
                pool_rstd(pool, t, 1)
                pool_rstd(pool, t + 3, 0)
            for t in range(NT - 3, NT):
                pool_rstd(pool, t, 1)
            pool.wait_ge(s["qk_loaded"], 32)
            pool_wqk(pool, 0, 1)
            pool_pair(pool, 0, first=True)
            with pool.Fori(1, PAIRS - 1) as p:
                pool_pair(pool, p)
            pool_pair(pool, PAIRS - 1, final=True)
            with pool.Fori(0, NT) as t:
                pool_rstd(pool, t + NT, 0)

        @block.tensor
        def _(pe):
            pe.wait_ge(s["warm_zeroed"], 1)
            for _ in range(WARM):
                nc.tensor.matmul(lb[:, 0:P], xa[:, 0:P], xa[:, 0:P], start=True, stop=True)
            pe.wait_ge(s["consts_ready"], 1)
            pe_ffn_transpose(pe, 0)

            pe_ffn_up_first(pe)
            pe_ffn_transpose(pe, 1)
            pe_ffn_gated_transpose(pe, 0)
            pe_ffn_up(pe, 1)
            pe_ffn_transpose(pe, 2)
            pe_ffn_down(pe, 0, first=True)
            pe_ffn_gated_transpose(pe, 1)
            pe_ffn_up(pe, 2)
            pe_ffn_transpose(pe, 3)
            pe_att_transpose(pe, 0, first=True)
            pe_ffn_down(pe, 1)
            with pe.Fori(3, NT - 1) as t:
                pe_ffn_gated_transpose(pe, t - 1)
                pe_ffn_up(pe, t)
                pe_ffn_transpose(pe, t + 1)
                pe_att_transpose(pe, t - 2)
                pe_ffn_down(pe, t - 1)
            pe_ffn_gated_transpose(pe, NT - 2)
            pe_ffn_up(pe, NT - 1)
            pe_att_transpose(pe, NT - 3)
            pe_ffn_down(pe, NT - 2)
            pe_ffn_gated_transpose(pe, NT - 1)
            pe.wait_ge(s["wqk0_split"], 1)
            pe_project(pe, 0, 0, qp, s["q_ready"])
            pe_att_transpose(pe, NT - 2)
            pe_ffn_down(pe, NT - 1)
            pe.wait_ge(s["wv_split"], 1)
            pe_value(pe, 0, 0, 0, wait_bank=False)
            pe.wait_ge(s["combined"], NT)
            pe_project(pe, 0, 1, kp, s["k_ready"])
            pe_att_transpose(pe, NT - 1)
            pe_value(pe, 0, 1, 1, wait_bank=False)
            pe_pair(pe, 0, first=True)
            with pe.Fori(1, PAIRS - 1) as p:
                pe_pair(pe, p)
            pe_pair(pe, PAIRS - 1, final=True)
            used = fill_before(PAIRS - 1, 3, False) - 2 + 4
            pe_ffn_transpose(pe, NT)
            pe.wait_ge(s["av_split"], 4 * PAIRS)
            for i in range(TH):
                pe_output(pe, 1, i, used + i)
            pe_ffn_up(pe, NT, used=used + TH)
            pe_ffn_transpose(pe, NT + 1)
            with pe.Fori(1, NT - 1) as t:
                pe_ffn_gated_transpose(pe, t + NT - 1)
                pe_ffn_up(pe, t + NT)
                pe_ffn_transpose(pe, t + NT + 1)
                pe_ffn_down(pe, t + NT - 1)
            pe_ffn_gated_transpose(pe, 2 * NT - 2)
            pe_ffn_up(pe, 2 * NT - 1)
            pe_ffn_down(pe, 2 * NT - 2)
            pe_ffn_gated_transpose(pe, 2 * NT - 1)
            pe_ffn_down(pe, 2 * NT - 1, dst=lb, last_tile=True)

        @block.scalar
        def _(act):
            for k in range(KD):
                act.wait_ge(up_loaded[k], 16)
                act_copy(upT_hi[:, k, :], upT_raw[:, k, :]).then_inc(s["up_hi"], 1)
                if k == 0:
                    act_ffn_transposed(act, 0)
            act_down_hi(act, 0)
            act_down_hi(act, 1)
            act_gate_exp(act, 0)
            act_ffn_transposed(act, 1)
            act_down_hi(act, 2)
            act_down_hi(act, 3)
            act_gated_transposed(act, 0)
            act_gate_exp(act, 1)
            act_ffn_transposed(act, 2)
            act_gated_transposed(act, 1)
            act_gate_exp(act, 2)
            act_ffn_transposed(act, 3)
            act_att_transposed(act, 0)
            with act.Fori(3, NT - 1) as t:
                act_gated_transposed(act, t - 1)
                act_gate_exp(act, t)
                act_ffn_transposed(act, t + 1)
                act_att_transposed(act, t - 2)
            act_gated_transposed(act, NT - 2)
            act_gate_exp(act, NT - 1)
            act_att_transposed(act, NT - 3)
            act_gated_transposed(act, NT - 1)
            act_q(act, 0, 0)
            act_att_transposed(act, NT - 2)
            act_value(act, 0, 0, 0)
            act_k(act, 0, 0)
            act_att_transposed(act, NT - 1)
            act_value(act, 0, 1, 1)
            act_pair(act, 0, first=True)
            with act.Fori(1, PAIRS - 1) as p:
                act_pair(act, p)
            act_pair(act, PAIRS - 1, final=True)
            act_ffn_transposed(act, NT)
            act_gate_exp(act, NT)
            act_ffn_transposed(act, NT + 1)
            with act.Fori(1, NT - 1) as t:
                act_gated_transposed(act, t + NT - 1)
                act_gate_exp(act, t + NT)
                act_ffn_transposed(act, t + NT + 1)
            act_gated_transposed(act, 2 * NT - 2)
            act_gate_exp(act, 2 * NT - 1)
            act_gated_transposed(act, 2 * NT - 1)

        @block.vector
        def _(dve):
            dve.wait_ge(s["x0_loaded"], 16)
            dve_stats(dve, 0, 0, x[:, 0, :])
            dve_normalise(dve, 0, 0, x[:, 0, :])
            for k in range(KD):
                dve.wait_ge(s["up_hi"], k + 1)
                nc.vector.tensor_tensor(upT_lo[:, k, :], upT_raw[:, k, :], upT_hi[:, k, :].bitcast(F32),
                                        ALU.subtract).then_inc(s["up_split"], 1)
                if k == 0:
                    dve_ffn_transposed(dve, 0)
                if k == KD - 2:
                    dve.wait_ge(s["x1_loaded"], 16)
                    dve_stats(dve, 1, 0, x[:, 1, :])

            def step(t, n, att=True, last=False, early=False, stats=True):
                if not last and stats:
                    dve_stats(dve, n + 1, 0, xt(t + 1))
                if not early:
                    dve_gated_transposed(dve, n - 1)
                    dve_gate_inverse(dve, n - 1)
                if not last:
                    dve_normalise(dve, n + 1, 0, xt(t + 1))
                if att:
                    dve_normalise(dve, t - 2, 1, xt(t - 2))
                dve_route(dve, n)
                if not last:
                    dve_ffn_transposed(dve, n + 1)
                if att:
                    dve_att_transposed(dve, t - 2)
                if not early:
                    dve_combine(dve, n - 1, t - 1)

            def stats_after(t):
                wait_alone(dve, s["combined"], t + 1)
                dve_stats(dve, t, 1, xt(t))
            step(0, 0, att=False, early=True, stats=False)
            dve.wait_ge(s["xr_loaded"], 16)
            step(1, 1, att=False)
            stats_after(0)
            step(2, 2)
            stats_after(1)
            with dve.Fori(3, NT - 1) as t:
                step(t, t)
                stats_after(t - 1)
            step(NT - 1, NT - 1, last=True)
            stats_after(NT - 2)
            dve_gated_transposed(dve, NT - 1)
            dve_gate_inverse(dve, NT - 1)
            dve_normalise(dve, NT - 2, 1, x[:, NT - 2, :])
            dve_q(dve, 0, 0)
            dve_att_transposed(dve, NT - 2)
            dve_combine(dve, NT - 1, NT - 1)
            stats_after(NT - 1)
            dve_normalise(dve, NT - 1, 1, x[:, NT - 1, :])
            dve_value(dve, 0, 0, 0)
            dve_k(dve, 0, 0)
            dve_att_transposed(dve, NT - 1)
            dve_value(dve, 0, 1, 1)
            dve.wait_ge(s["consts_ready"], 3)
            dve_pair(dve, 0, first=True)
            with dve.Fori(1, PAIRS - 1) as p:
                dve_pair(dve, p)
            dve_pair(dve, PAIRS - 1, final=True)
            used = fill_before(PAIRS - 1, 3, False) - 2 + 4
            dve_ffn_transposed(dve, NT)
            for i in range(TH):
                dve_output(dve, 1, i, used + i)
            dve.wait_ge(s["fill_done"], used + TH)
            step(0, NT, att=False, early=True)
            with dve.Fori(1, NT - 1) as t:
                step(t, t + NT, att=False)
            step(NT - 1, 2 * NT - 1, att=False, last=True)
            dve_gated_transposed(dve, 2 * NT - 1)
            dve_gate_inverse(dve, 2 * NT - 1)
            dve_combine(dve, 2 * NT - 1, NT - 1, src=lb)


def kernel(L0_attn_hidden_states, L0_attn_wq, L0_attn_wkv, L0_attn_wo, L0_ffn_A, L0_ffn_B, L0_ffn_Wr):
    import numpy as np
    import concourse.bacc as bacc
    from concourse.bass_utils import run_bass_kernel_spmd

    hidden = np.asarray(L0_attn_hidden_states)
    a, b, wr = (np.asarray(v) for v in (L0_ffn_A, L0_ffn_B, L0_ffn_Wr))
    wq, wkv, wo = (np.asarray(v) for v in (L0_attn_wq, L0_attn_wkv, L0_attn_wo))

    up = np.concatenate([wr, a.reshape(KR, D)], axis=0).T.reshape(KD, P, UPW).transpose(1, 0, 2)
    down = b.transpose(0, 2, 1).reshape(NR, P, D).transpose(1, 0, 2)
    q = wq.reshape(KD, P, HEADS, wq.shape[1] // HEADS)[..., :DH]
    k = wkv[:, :HEADS * DH].reshape(KD, P, HEADS, DH)
    qk = np.stack([q, k]).transpose(3, 2, 0, 1, 4).reshape(HEADS, P, 2 * D)
    v = wkv[:, HEADS * DH:2 * HEADS * DH].reshape(KD, P, PAIRS, 2 * DH).transpose(2, 1, 0, 3).reshape(PAIRS, P, 2 * D)
    o = wo.reshape(PAIRS, 2, DH, D).transpose(0, 2, 1, 3).reshape(PAIRS, P, 2 * D)
    arrays = {"x_in": hidden.reshape(NT, P, D), "up_w": up, "down_w": down, "wqk": qk, "wv": v, "wo": o}
    arrays = {n: np.ascontiguousarray(v) for n, v in arrays.items()}

    nc = bacc.Bacc("TRN2", target_bir_lowering=False, num_devices=1, dynamic_dma_scratch_size=1024)
    aps = [nc.dram_tensor(n, v.shape, F32, kind="ExternalInput").ap() for n, v in arrays.items()]
    out = nc.dram_tensor("out", [NT, P, D], F32, kind="ExternalOutput").ap()
    build_macaron(nc, *aps, out)
    result = run_bass_kernel_spmd(nc, [arrays], core_ids=[0])
    return result.results[0]["out"].reshape(hidden.shape)
```
